# Optimizing a Trainium2 kernel written in Bass

```python
import numpy as np
import jax
import jax.numpy as jnp

def _softmax(x, axis=-1):
    return jax.nn.softmax(x, axis=axis)

def _gelu(x):
    return jax.nn.gelu(x, approximate=True)

def _silu(x):
    return jax.nn.silu(x)

def _sigmoid(x):
    return jax.nn.sigmoid(x)

def _layernorm(x, axis=-1, eps=1e-05):
    m = jnp.mean(x, axis=axis, keepdims=True)
    v = jnp.var(x, axis=axis, keepdims=True)
    return (x - m) / jnp.sqrt(v + eps)

def _scatter_add(tgt, idx, src, axis=0):
    return tgt.at[idx].add(src)

def _segment_sum(src, seg, n):
    return jax.ops.segment_sum(src, seg, n)
kernel_name = 'mk_adj_ffn_d1_adj_r2_c61a5a'

def setup_inputs(seed: int=0):
    np.random.seed(seed)
    _w = jnp.asarray

    def _rec_inputs():
        import jax
        import jax.numpy as jnp
        _gk = jax.random.key(seed)
        x = -0.0002928 + 1 * jax.random.normal(jax.random.fold_in(_gk, 1), (8, 1024, 128), jnp.float32)
        _a = jax.random.bernoulli(jax.random.fold_in(_gk, 2), 0.00195312, (8, 1024, 1024))
        _a = jnp.logical_or(_a, jnp.swapaxes(_a, -1, -2))
        _a = jnp.logical_or(_a, jnp.eye(1024, dtype=bool))
        adj = _a.astype(jnp.int32)
        return (x, adj)
    x, adj = _rec_inputs()

    def _L0_gnn_setup():
        import jax, jax.numpy as jnp
        import numpy as np
        NEG_INF = -1000000000.0
        LEAKY_SLOPE = 0.2
        key = jax.random.key(seed)
        k1, k2, k3, k4 = jax.random.split(key, 4)
        B, N, D_in, D_out = (8, 1024, 128, 128)
        x = jax.random.normal(k1, (B, N, D_in), dtype=jnp.float32)
        adj_matrix = jax.random.randint(k2, (B, N, N), 0, 2, dtype=jnp.int32)
        W = jax.random.normal(k3, (D_out, D_in), dtype=jnp.float32) / np.sqrt(D_in)
        a = jax.random.normal(k4, (1, 2 * D_out), dtype=jnp.float32) / np.sqrt(2 * D_out)
        return {'x': x, 'adj_matrix': adj_matrix, 'W': W, 'a': a}
    _L0_gnn_all = _L0_gnn_setup()
    _L0_gnn_in = {k: v for k, v in _L0_gnn_all.items() if k in ('W', 'a')}
    del _L0_gnn_all

    def _L0_ffn_setup():
        import jax, jax.numpy as jnp
        import numpy as np
        BN_EPS = 0.001

        def _bn(h, g, b, m, v):
            return g * (h - m) * jax.lax.rsqrt(v + BN_EPS) + b
        key = jax.random.key(seed)
        ks = jax.random.split(key, 8)
        B, F, Df = (128, 64, 128)
        E, H, D = (8, 128, 128)
        s1 = 1.0 / np.sqrt(Df)
        s2 = 1.0 / np.sqrt(H)
        return {'x': jax.random.normal(ks[0], (B, F, Df), jnp.float32), 'Wr': jax.random.normal(ks[1], (Df, E), jnp.float32) * s1, 'br': jnp.zeros((E,), jnp.float32), 'W1': jax.random.normal(ks[2], (E, Df, H), jnp.float32) * s1, 'b1': jnp.zeros((E, H), jnp.float32), 'g1': jnp.ones((E, H), jnp.float32), 'be1': jnp.zeros((E, H), jnp.float32), 'm1': jnp.zeros((E, H), jnp.float32), 'v1': jnp.ones((E, H), jnp.float32), 'W2': jax.random.normal(ks[3], (E, H, H), jnp.float32) * s2, 'b2': jnp.zeros((E, H), jnp.float32), 'g2': jnp.ones((E, H), jnp.float32), 'be2': jnp.zeros((E, H), jnp.float32), 'm2': jnp.zeros((E, H), jnp.float32), 'v2': jnp.ones((E, H), jnp.float32), 'Wo': jax.random.normal(ks[4], (E, H, D), jnp.float32) * s2, 'bo': jnp.zeros((E, D), jnp.float32)}
    _L0_ffn_all = _L0_ffn_setup()
    _L0_ffn_in = {k: v for k, v in _L0_ffn_all.items() if k in ('Wr', 'br', 'W1', 'b1', 'g1', 'be1', 'm1', 'v1', 'W2', 'b2', 'g2', 'be2', 'm2', 'v2', 'Wo', 'bo')}
    del _L0_ffn_all
    return {'x': x, 'adj': adj, 'L0_gnn_W': _L0_gnn_in['W'], 'L0_gnn_a': _L0_gnn_in['a'], 'L0_ffn_Wr': _L0_ffn_in['Wr'], 'L0_ffn_br': _L0_ffn_in['br'], 'L0_ffn_W1': _L0_ffn_in['W1'], 'L0_ffn_b1': _L0_ffn_in['b1'], 'L0_ffn_g1': _L0_ffn_in['g1'], 'L0_ffn_be1': _L0_ffn_in['be1'], 'L0_ffn_m1': _L0_ffn_in['m1'], 'L0_ffn_v1': _L0_ffn_in['v1'], 'L0_ffn_W2': _L0_ffn_in['W2'], 'L0_ffn_b2': _L0_ffn_in['b2'], 'L0_ffn_g2': _L0_ffn_in['g2'], 'L0_ffn_be2': _L0_ffn_in['be2'], 'L0_ffn_m2': _L0_ffn_in['m2'], 'L0_ffn_v2': _L0_ffn_in['v2'], 'L0_ffn_Wo': _L0_ffn_in['Wo'], 'L0_ffn_bo': _L0_ffn_in['bo']}

def reference(x, adj, L0_gnn_W, L0_gnn_a, L0_ffn_Wr, L0_ffn_br, L0_ffn_W1, L0_ffn_b1, L0_ffn_g1, L0_ffn_be1, L0_ffn_m1, L0_ffn_v1, L0_ffn_W2, L0_ffn_b2, L0_ffn_g2, L0_ffn_be2, L0_ffn_m2, L0_ffn_v2, L0_ffn_Wo, L0_ffn_bo):
    import jax
    import jax.numpy as jnp

    def _L0_gnn_ref(x, adj_matrix, W, a):
        import jax, jax.numpy as jnp
        import numpy as np
        NEG_INF = -1000000000.0
        LEAKY_SLOPE = 0.2
        h = jnp.einsum('bnd,od->bno', x, W)
        D = h.shape[-1]
        a_left, a_right = (a[0, :D], a[0, D:])
        e = (h @ a_left)[:, :, None] + (h @ a_right)[:, None, :]
        e = jnp.where(e > 0, e, LEAKY_SLOPE * e)
        e = jnp.where(adj_matrix == 0, NEG_INF, e)
        alpha = jax.nn.softmax(e, axis=-1)
        return jnp.einsum('bij,bjd->bid', alpha, h)

    def _L0_ffn_ref(x, Wr, br, W1, b1, g1, be1, m1, v1, W2, b2, g2, be2, m2, v2, Wo, bo):
        import jax, jax.numpy as jnp
        import numpy as np
        BN_EPS = 0.001

        def _bn(h, g, b, m, v):
            return g * (h - m) * jax.lax.rsqrt(v + BN_EPS) + b
        feat = jnp.mean(x, axis=0)
        w = jax.nn.softmax(feat @ Wr + br, axis=-1)
        h = jnp.einsum('bfd,edh->bfeh', x, W1) + b1
        h = jax.nn.relu(_bn(h, g1, be1, m1, v1))
        h = jnp.einsum('bfeh,ehk->bfek', h, W2) + b2
        h = jax.nn.relu(_bn(h, g2, be2, m2, v2))
        y = jnp.einsum('bfeh,ehd->bfed', h, Wo) + bo
        return jnp.einsum('bfed,fe->bfd', y, w)
    x = x + _L0_gnn_ref(_layernorm(x, axis=-1), adj, L0_gnn_W, L0_gnn_a)
    x = x + _L0_ffn_ref(_layernorm(x, axis=-1), L0_ffn_Wr, L0_ffn_br, L0_ffn_W1, L0_ffn_b1, L0_ffn_g1, L0_ffn_be1, L0_ffn_m1, L0_ffn_v1, L0_ffn_W2, L0_ffn_b2, L0_ffn_g2, L0_ffn_be2, L0_ffn_m2, L0_ffn_v2, L0_ffn_Wo, L0_ffn_bo)
    return x

_drawn_inputs = setup_inputs


def setup_inputs(seed=0):
    import zlib

    import numpy as np

    out = dict(_drawn_inputs(seed))
    spreads = {'L0_ffn_br': (0.0, 0.302),
     'L0_ffn_b1': (0.0, 0.461),
     'L0_ffn_g1': (1.0, 0.2),
     'L0_ffn_be1': (0.0, 0.474),
     'L0_ffn_m1': (0.0, 0.454),
     'L0_ffn_v1': (1.0, 0.6),
     'L0_ffn_b2': (0.0, 0.333),
     'L0_ffn_g2': (1.0, 0.2),
     'L0_ffn_be2': (0.0, 0.353),
     'L0_ffn_m2': (0.0, 0.342),
     'L0_ffn_v2': (1.0, 0.6),
     'L0_ffn_bo': (0.0, 0.1)}
    factors = {}
    for name, (base, spread) in spreads.items():
        noise = np.random.default_rng([zlib.crc32(name.encode()), seed]).standard_normal(out[name].shape)
        drawn = base * np.exp(spread * noise) if base else spread * noise
        out[name] = jnp.asarray(drawn.astype(out[name].dtype))
    for name, factor in factors.items():
        out[name] = (out[name] * factor).astype(out[name].dtype)
    return out
```

```python
from contextlib import ExitStack

import concourse.bass as bass
from concourse import mybir

P = 128
F32 = mybir.dt.float32
F32R = mybir.dt.float32r
BF16 = mybir.dt.bfloat16
I32 = mybir.dt.int32
ALU = mybir.AluOpType
ACT = mybir.ActivationFunctionType
AX_X = mybir.AxisListType.X

LN_EPS = 1e-5
BN_EPS = 1e-3
SLOPE = 0.2
MASKED = 1e30
LAG = 3


def gat_moe(nc, x, adj, gnn_W, gnn_a, Wr, br, W1, b1, g1, be1, m1, v1, W2, b2, g2, be2, m2, v2, Wo, bo, out):
    B, N, D = x.shape
    E, _, H = W1.shape
    U = N // P
    NT = N // P
    assert B == 8 and U == 8 and E == 8 and D == P and H == P
    TOK = B * P
    HALF = TOK // 2

    x_tiles = x.rearrange("b (t p) d -> b p t d", p=P)
    out_groups = out.rearrange("b (t p) d -> t p b d", p=P)

    ctx = ExitStack()
    with ctx:
        def sb(name, shape, dt=F32):
            return ctx.enter_context(nc.sbuf_tensor(name, shape, dt))

        def sem(name):
            return ctx.enter_context(nc.semaphore(name))

        ident = sb("ident", [P, P])
        ones_row = sb("ones_row", [P, P])
        minus_half = sb("minus_half", [P, 2 * E])
        neg_r = sb("neg_r", [P, B, N])
        neg_r02 = sb("neg_r02", [P, B, N])
        neg_l08 = sb("neg_l08", [P, B * U])
        h_all = sb("h_all", [P, B, NT, D])
        adj_t = sb("adj_t", [P, 2, N], I32)
        x_t = sb("x_t", [P, 4, D])
        mask = sb("mask", [P, N], BF16)
        score = sb("score", [P, N])
        probs = sb("probs", [P, N])
        probsT = sb("probsT", [P, NT, P])
        row_min = sb("row_min", [P, 2])
        row_sum = sb("row_sum", [P, 2])
        row_rcp = sb("row_rcp", [P, 2])
        x1 = sb("x1", [P, 3 * TOK])
        stats = sb("stats", [P, NT, 6])
        mean_var = sb("mean_var", [P, B, 2])
        var_eps = sb("var_eps", [P, B])
        rstd = sb("rstd", [P, B])
        xn_y = sb("xn_y", [P, TOK])
        xT_hi = sb("xT_hi", [P, TOK], F32R)
        xT_lo = sb("xT_lo", [P, TOK], F32R)
        a1 = sb("a1", [P, TOK])
        a1_hi = sb("a1_hi", [P, 2, TOK], F32R)
        a1_lo = sb("a1_lo", [P, 2, TOK], F32R)
        a2 = sb("a2", [P, 2, TOK])
        route_b = sb("route_b", [P, E, P])
        W1_hi = sb("W1_hi", [P, E * H], F32R)
        W1_lo = sb("W1_lo", [P, E * H], F32R)
        W2_hi = sb("W2_hi", [P, E * H], F32R)
        W2_lo = sb("W2_lo", [P, E * H], F32R)
        Wo_sb = sb("Wo_sb", [P, E, D])
        Wr_sb = sb("Wr_sb", [P, E])
        Wr_hi = sb("Wr_hi", [P, E], F32R)
        Wr_lo = sb("Wr_lo", [P, E], F32R)
        br_b = sb("br_b", [P, E])
        prm_rows = sb("prm_rows", [P, P])
        prm = sb("prm", [P, 10 * E])
        bn_s = sb("bn_s", [P, 2 * E])
        bn_t = sb("bn_t", [P, 2 * E])
        neg_t2 = sb("neg_t2", [P, E])
        t2_diag = sb("t2_diag", [P, E * E])
        bo_sb = sb("bo_sb", [E, D])
        y_const = sb("y_const", [E, D])
        W_sb = sb("W_sb", [P, D])
        a_cols = sb("a_cols", [P, 2])
        W_aug = sb("W_aug", [P, D + 2])
        wr_bc = sb("wr_bc", [P, P])
        logits = sb("logits", [P, E])
        logit_max = sb("logit_max", [P, 1])
        logit_off = sb("logit_off", [P, E])
        route_e = sb("route_e", [P, E])
        route_sum = sb("route_sum", [P, 1])
        route_rcp = sb("route_rcp", [P, 1])
        route = sb("route", [P, E])
        routeT = sb("routeT", [E, P])
        yc_T = sb("yc_T", [P, P])
        pro_x = a2
        pro_xn = xn_y
        pro_xnT = probs
        W1_raw = a1
        W2_raw = route_b

        bank = ctx.enter_context(nc.psum_tensor("bank", [P, 8, 512], F32))
        za = bank[:, 0:2, :].rearrange("p a n -> p (a n)")
        zb = bank[:, 2:4, :].rearrange("p a n -> p (a n)")
        yb = bank[:, 4:6, :].rearrange("p a n -> p (a n)")
        ptb = bank[:, 6, :]
        ob = bank[:, 7, :]
        pro_h = bank[:, 2:6, :].rearrange("p a (c n) -> p (a c) n", c=2)
        pro_r = bank[:, 6:8, :].rearrange("p a n -> p (a n)")

        adj_loaded = [sem(f"adj_loaded{i}") for i in range(2)]
        xt_loaded = [sem(f"xt_loaded{i}") for i in range(4)]
        prox_loaded = [sem(f"prox_loaded{i}") for i in range(2)]
        gnn_loaded = sem("gnn_loaded")
        prm_loaded = sem("prm_loaded")
        w_loaded = sem("w_loaded")
        stored = sem("stored")
        consts = sem("consts")
        ident_ready = sem("ident_ready")
        rows_clear = sem("rows_clear")
        WT_psum = sem("WT_psum")
        WT_ready = sem("WT_ready")
        wl_psum = sem("wl_psum")
        wl_ready = sem("wl_ready")
        prm_psum = sem("prm_psum")
        prm_ready = sem("prm_ready")
        bnv_ready = sem("bnv_ready")
        bnr_ready = sem("bnr_ready")
        bn_step = sem("bn_step")
        s2_psum = sem("s2_psum")
        wsplit = sem("wsplit")
        yc_psum = sem("yc_psum")
        yc_ready = sem("yc_ready")
        pst = sem("pst")
        pag = sem("pag")
        pve = sem("pve")
        prs = sem("prs")
        pxn = sem("pxn")
        pT = sem("pT")
        pTc = sem("pTc")
        ph = sem("ph")
        phc = sem("phc")
        pl = sem("pl")
        pr = sem("pr")
        prc = sem("prc")
        pr02 = sem("pr02")
        mask_ready = sem("mask_ready")
        e_ready = sem("e_ready")
        score_ready = sem("score_ready")
        p_ready = sem("p_ready")
        rcp_ready = sem("rcp_ready")
        pt_psum = sem("pt_psum")
        pt_copied = sem("pt_copied")
        o_ready = sem("o_ready")
        x1_ready = sem("x1_ready")
        stats_ready = sem("stats_ready")
        mv_ready = sem("mv_ready")
        var_ready = sem("var_ready")
        rstd_ready = sem("rstd_ready")
        xn_ready = sem("xn_ready")
        xT_psum = sem("xT_psum")
        xhi_ready = sem("xhi_ready")
        xlo_ready = sem("xlo_ready")
        lg_psum = sem("lg_psum")
        lg_ready = sem("lg_ready")
        lmax_ready = sem("lmax_ready")
        loff_ready = sem("loff_ready")
        re_ready = sem("re_ready")
        rr_ready = sem("rr_ready")
        route_ready = sem("route_ready")
        rb_psum = sem("rb_psum")
        rb_ready = sem("rb_ready")
        rT_psum = sem("rT_psum")
        rT_ready = sem("rT_ready")
        yc2_psum = sem("yc2_psum")
        yc2_ready = sem("yc2_ready")
        y_ready = sem("y_ready")
        yT_psum = sem("yT_psum")
        out_ready = sem("out_ready")
        z1_ready = sem("z1_ready")
        a1_ready = sem("a1_ready")
        hi1_ready = sem("hi1_ready")
        lo1_ready = sem("lo1_ready")
        z2_ready = sem("z2_ready")
        a2_ready = sem("a2_ready")
        z3_done = sem("z3_done")

        def runs(first, last, v):
            return not isinstance(v, int) or first <= v <= last

        def turn(u, s, lag):
            return (u - 1, s - lag) if s >= lag else (u - 2, s - lag + E)

        def await_turns(eng, semaphore, value):
            if not isinstance(value, int) or value > 0:
                eng.wait_ge(semaphore, value)

        def over_groups(eng, body, last):
            body(0)
            body(1)
            with eng.Fori(2, U) as u:
                body(u)
            for u in range(U, last + 1):
                body(u)

        block = ctx.enter_context(nc.Block())

        @block.sync
        def _(sp):
            def load_tile(u, s, wait):
                n = 8 * u + s
                if wait:
                    sp.wait_ge(mask_ready, n - 1)
                sp.dma_start(adj_t[:, s % 2, :], adj[s, bass.ds(u * P, P), :]).then_inc(adj_loaded[s % 2], 16)
                if not isinstance(n, int) or n >= 4:
                    sp.wait_ge(x1_ready, n - 3)
                sp.dma_start(x_t[:, s % 4, :], x[s, bass.ds(u * P, P), :]).then_inc(xt_loaded[s % 4], 16)

            def load_batch(b):
                if b >= 2:
                    sp.wait_ge(pxn, b - 1)
                sp.dma_start(pro_x[:, b % 2, :].rearrange("p (t d) -> p t d", d=D), x_tiles[b]).then_inc(
                    prox_loaded[b % 2], 16)

            load_batch(0)
            sp.sem_inc(stored, 16)
            sp.dma_start(W_sb[:], gnn_W).then_inc(gnn_loaded, 16)
            sp.dma_start(a_cols[:], gnn_a.rearrange("o (c p) -> p (o c)", c=2), allow_slow_non_contiguous=True).then_inc(gnn_loaded, 16)
            load_batch(1)
            sp.wait_ge(rows_clear, 1)
            for i, v in enumerate((v1, v2, g1, g2, b1, b2, m1, m2, be1, be2)):
                sp.dma_start(prm_rows[i * E:(i + 1) * E, :], v).then_inc(prm_loaded, 16)
            sp.dma_start(W1_raw[:].rearrange("p (e h) -> p e h", e=E), W1.rearrange("e d h -> d e h")).then_inc(w_loaded, 16)
            sp.dma_start(W2_raw[:], W2.rearrange("e d h -> d e h")).then_inc(w_loaded, 16)
            sp.dma_start(Wo_sb[:], Wo.rearrange("e h d -> h e d")).then_inc(w_loaded, 16)
            sp.dma_start(Wr_sb[:], Wr).then_inc(w_loaded, 16)
            sp.dma_start(br_b[:], br.partition_broadcast(P)).then_inc(w_loaded, 16)
            sp.dma_start(bo_sb[:], bo).then_inc(w_loaded, 16)
            for s in range(2):
                load_tile(0, s, False)
            for b in range(2, B):
                load_batch(b)
            for s in range(2, 8):
                load_tile(0, s, True)

            def store(g):
                sp.wait_ge(out_ready, g + 1)
                slot = x1[:, bass.ds((g % 3) * TOK, TOK)].rearrange("p (b d) -> p b d", b=B)
                sp.dma_start(out_groups[g] if isinstance(g, int) else
                             out_groups[bass.ds(g, 1)].rearrange("t p b d -> (t p) b d"), slot).then_inc(stored, 16)

            for s in range(8):
                load_tile(1, s, True)
            with sp.Fori(2, U) as u:
                for s in range(8):
                    load_tile(u, s, True)
                store(u - 2)
            store(U - 2)
            store(U - 1)
            sp.wait_ge(stored, 16 * (U + 1))

        @block.gpsimd
        def _(pool):
            nc.gpsimd.memset(ident[:], 0.0).then_inc(consts, 1)
            nc.gpsimd.memset(minus_half[:], -0.5).then_inc(consts, 1)
            nc.gpsimd.memset(ones_row[:], 1.0).then_inc(consts, 1)
            nc.gpsimd.memset(prm_rows[:], 0.0).then_inc(rows_clear, 1)
            pool.wait_ge(consts, 1)
            nc.gpsimd.affine_select(out=ident[:], in_=ident[:], compare_op=ALU.not_equal, fill=1.0, base=0,
                                    pattern=[[-1, P]], channel_multiplier=1).then_inc(ident_ready, 1)
            pool.wait_ge(consts, 3)
            for b in range(B):
                pool.wait_ge(pve, b + 1)
                if b >= 1:
                    pool.wait_ge(pxn, b)
                nc.gpsimd.tensor_tensor(rstd[:], var_eps[:], minus_half[:, 0:NT], ALU.pow).then_inc(prs, 1)
            pool.wait_ge(bnv_ready, 1)
            nc.gpsimd.tensor_tensor(bn_s[:], bn_t[:], minus_half[:], ALU.pow).then_inc(bnr_ready, 1)

            def group_rstd(g):
                pool.wait_ge(var_ready, g + 1)
                if isinstance(g, int):
                    pool.wait_ge(pxn, B)
                else:
                    pool.wait_ge(xn_ready, g)
                nc.gpsimd.tensor_tensor(rstd[:], var_eps[:], minus_half[:, 0:B], ALU.pow).then_inc(rstd_ready, 1)

            group_rstd(0)
            with pool.Fori(1, U) as g:
                group_rstd(g)

        @block.scalar
        def _(act):
            for b in range(B):
                act.wait_ge(pT, b + 1)
                if b >= 1:
                    act.wait_ge(pr, b)
                nc.scalar.activation(pro_xnT[:], za, ACT.Copy).then_inc(pTc, 1)
                act.wait_ge(ph, b + 1)
                nc.scalar.activation(h_all[:, b], pro_h[:, :, 0:D], ACT.Copy).then_inc(phc, 1)
                act.wait_ge(pr, b + 1)
                nc.scalar.activation(neg_r[:, b], pro_r, ACT.Copy, scale=-1.0).then_inc(prc, 1)

            def relu1(u, s):
                g, e = turn(u, s, LAG)
                if not runs(0, U - 1, g):
                    return
                k = E * g + e
                act.wait_ge(z1_ready, k + 1)
                await_turns(act, lo1_ready, k)
                nc.scalar.activation(a1[:], za, ACT.Relu, bias=bn_t[:, e:e + 1], scale=bn_s[:, e:e + 1]).then_inc(a1_ready, 1)

            def hi1(u, s):
                g, e = turn(u, s, LAG)
                if not runs(0, U - 1, g):
                    return
                k = E * g + e
                act.wait_ge(a1_ready, k + 1)
                await_turns(act, z2_ready, k - 1)
                nc.scalar.activation(a1_hi[:, e % 2], a1[:], ACT.Copy).then_inc(hi1_ready, 1)

            def copy_pT(u, s, half):
                b = (s - 1) % 8
                m = 8 * u + s - 1
                if not runs(0, 8 * U - 1, m):
                    return
                act.wait_ge(pt_psum, 2 * m + half + 1)
                if half == 0:
                    await_turns(act, o_ready, m)
                nc.scalar.activation(probsT[:, 4 * half:4 * half + 4].rearrange("p t i -> p (t i)"), ptb, ACT.Copy).then_inc(pt_copied, 1)

            def iteration(u):
                for s in range(8):
                    n = 8 * u + s
                    g = u - 1
                    if isinstance(u, int) and u > U and s > 5:
                        break
                    if s == LAG + 1 and runs(0, U - 1, g):
                        act.wait_ge(loff_ready, g + 1)
                        nc.scalar.activation(route_e[:], logit_off[:], ACT.Exp, accum_out=route_sum[:]).then_inc(re_ready, 1)
                    relu1(u, s)
                    copy_pT(u, s, 0)
                    hi1(u, s)
                    copy_pT(u, s, 1)
                    if s == LAG - 1 and runs(0, U - 1, g):
                        act.wait_ge(xT_psum, g + 1)
                        nc.scalar.activation(xT_hi[:], za, ACT.Copy).then_inc(xhi_ready, 1)
                    if s == LAG + 1 and runs(0, U - 1, g):
                        act.wait_ge(rb_psum, g + 1)
                        await_turns(act, a2_ready, 8 * g)
                        nc.scalar.activation(route_b[:].rearrange("p e f -> p (e f)"), za, ACT.Copy).then_inc(rb_ready, 1)
                    if runs(0, U - 1, u):
                        act.wait_ge(score_ready, n + 1)
                        await_turns(act, pt_psum, 2 * n)
                        nc.scalar.activation(probs[:], score[:], ACT.Exp, bias=row_min[:, s % 2:s % 2 + 1], scale=-1.0,
                                             accum_out=row_sum[:, s % 2:s % 2 + 1]).then_inc(p_ready, 1)

            over_groups(act, iteration, U + 1)

        @block.vector
        def _(dve):
            v = nc.vector
            dve.wait_ge(WT_psum, 1)
            v.tensor_copy(W_aug[:, 0:D], bank[:, 6, 0:D]).then_inc(WT_ready, 1)
            dve.wait_ge(wl_psum, 1)
            v.tensor_copy(W_aug[:, D:D + 2], bank[:, 0, 0:2]).then_inc(wl_ready, 1)
            v.tensor_copy(wr_bc[:], bank[:, 1, 0:P]).then_inc(wl_ready, 1)
            for b in range(B):
                xb = pro_x[:, b % 2, :].rearrange("p (t d) -> p t d", d=D)
                xn = pro_xn[:].rearrange("p (t d) -> p t d", d=D)
                dve.wait_ge(prox_loaded[b % 2], 16 * (b // 2 + 1))
                for t in range(NT):
                    last = v.bn_stats(stats[:, t, :], xb[:, t, :])
                last.then_inc(pst, 1)
                dve.wait_ge(pst, b + 1)
                if b >= 1:
                    dve.wait_ge(pxn, b)
                for t in range(NT):
                    last = v.bn_aggr(mean_var[:, t, :], stats[:, t, :])
                last.then_inc(pag, 1)
                dve.wait_ge(pag, b + 1)
                v.tensor_scalar(var_eps[:], mean_var[:, :, 1], LN_EPS, None, ALU.add).then_inc(pve, 1)
                if b >= 1:
                    dve.wait_ge(phc, b)
                    v.tensor_scalar(neg_l08[:, (b - 1) * U:b * U], pro_h[:, :, D], -(1.0 - SLOPE), None, ALU.mult).then_inc(pl, 1)
                    dve.wait_ge(prc, b)
                    v.tensor_scalar(neg_r02[:, b - 1], neg_r[:, b - 1], SLOPE, None, ALU.mult).then_inc(pr02, 1)
                    dve.wait_ge(pT, b)
                dve.wait_ge(prs, b + 1)
                for t in range(NT):
                    last = v.tensor_scalar(xn[:, t, :], xb[:, t, :], mean_var[:, t, 0:1], rstd[:, t:t + 1],
                                           ALU.subtract, ALU.mult)
                last.then_inc(pxn, 1)
            dve.wait_ge(phc, B)
            v.tensor_scalar(neg_l08[:, (B - 1) * U:B * U], pro_h[:, :, D], -(1.0 - SLOPE), None, ALU.mult).then_inc(pl, 1)
            dve.wait_ge(prc, B)
            v.tensor_scalar(neg_r02[:, B - 1], neg_r[:, B - 1], SLOPE, None, ALU.mult).then_inc(pr02, 1)

            dve.wait_ge(pxn, B)

            dve.wait_ge(prm_psum, 1)
            v.tensor_copy(prm[:], bank[:, 1, 0:10 * E]).then_inc(prm_ready, 1)
            dve.wait_ge(prm_ready, 1)
            v.tensor_scalar(bn_t[:], prm[:, 0:2 * E], BN_EPS, None, ALU.add).then_inc(bnv_ready, 1)
            dve.wait_ge(bnr_ready, 1)
            pair = [prm[:, 2 * E * i:2 * E * (i + 1)] for i in range(5)]
            v.tensor_tensor(bn_s[:], bn_s[:], pair[1], ALU.mult).then_inc(bn_step, 1)
            v.tensor_tensor(bn_t[:], pair[2], pair[3], ALU.subtract).then_inc(bn_step, 1)
            dve.wait_ge(bn_step, 2)
            v.tensor_tensor(bn_t[:], bn_t[:], bn_s[:], ALU.mult).then_inc(bn_step, 1)
            v.memset(t2_diag[:], 0.0).then_inc(bn_step, 1)
            dve.wait_ge(bn_step, 4)
            v.tensor_tensor(bn_t[:], bn_t[:], pair[4], ALU.add).then_inc(bn_step, 1)
            dve.wait_ge(bn_step, 5)
            v.tensor_scalar(neg_t2[:], bn_t[:, E:2 * E], -1.0, None, ALU.mult).then_inc(bn_step, 1)
            v.tensor_copy(t2_diag[:, 0:E * E:E + 1], bn_t[:, E:2 * E]).then_inc(bn_step, 1)
            dve.wait_ge(w_loaded, 16 * 6)
            v.tensor_copy(W1_hi[:], W1_raw[:])
            v.tensor_copy(Wr_hi[:], Wr_sb[:])
            w2 = W2_raw[:].rearrange("p e h -> p (e h)")
            dve.wait_ge(s2_psum, 1)
            v.tensor_tensor(w2, w2, pro_r, ALU.mult).then_inc(wsplit, 1)
            dve.wait_ge(wsplit, 1)
            v.tensor_copy(W2_hi[:], w2).then_inc(wsplit, 1)
            dve.wait_ge(wsplit, 2)
            v.tensor_tensor(W1_lo[:], W1_raw[:], W1_hi[:].bitcast(F32), ALU.subtract)
            v.tensor_tensor(Wr_lo[:], Wr_sb[:], Wr_hi[:].bitcast(F32), ALU.subtract)
            v.tensor_tensor(W2_lo[:], w2, W2_hi[:].bitcast(F32), ALU.subtract).then_inc(wsplit, 1)
            dve.wait_ge(yc_psum, 1)
            v.tensor_copy(y_const[:], bank[0:E, 0, 0:D]).then_inc(yc_ready, 1)

            def x1_tile(um, b):
                return x1[:, bass.ds((um % 3) * TOK + b * D, D)]

            def iteration(u):
                for s in range(8):
                    if isinstance(u, int) and u > U and s > 5:
                        break
                    g = u - 1
                    n = 8 * u + s
                    live = runs(0, U - 1, u)
                    c = s % 2
                    um, b2_ = (u, s - 2) if s >= 2 else (u - 1, s + 6)
                    m2_ = 8 * u + s - 2
                    old = runs(0, 8 * U - 1, m2_)
                    if s == LAG - 1 and runs(0, U - 1, g):
                        dve.wait_ge(rstd_ready, g + 1)
                        for b in range(B):
                            last = v.tensor_scalar(xn_y[:, b * D:(b + 1) * D], x1_tile(g, b), mean_var[:, b, 0:1],
                                                   rstd[:, b:b + 1], ALU.subtract, ALU.mult)
                        last.then_inc(xn_ready, 1)
                    if old:
                        dve.wait_ge(o_ready, m2_ + 1)
                        dve.wait_ge(rcp_ready, m2_ + 1)
                        dve.wait_ge(xt_loaded[b2_ % 4], 16 * (2 * um + b2_ // 4 + 1))
                        if b2_ == 0 and runs(3, U - 1, um):
                            dve.wait_ge(stored, 16 * (um - 1))
                        v.scalar_tensor_tensor(x1_tile(um, b2_), ob[:, 0:D], row_rcp[:, c:c + 1], x_t[:, b2_ % 4, :],
                                               ALU.mult, ALU.add).then_inc(x1_ready, 1)
                    if old:
                        dve.wait_ge(x1_ready, m2_ + 1)
                        await_turns(dve, mv_ready, m2_)
                        if b2_ == 0:
                            await_turns(dve, xn_ready, um)
                    if live:
                        dve.wait_ge(adj_loaded[c], 16 * (4 * u + s // 2 + 1))
                        await_turns(dve, score_ready, n)
                        v.tensor_scalar(mask[:], adj_t[:, c, :], 0.0, MASKED, ALU.is_equal, ALU.mult).then_inc(mask_ready, 1)
                    if old:
                        v.bn_stats(stats[:, 0, :], x1_tile(um, b2_)).then_inc(stats_ready, 1)
                        dve.wait_ge(stats_ready, m2_ + 1)
                    if live:
                        await_turns(dve, p_ready, n)
                        v.scalar_tensor_tensor(score[:], neg_r[:, s], neg_l08[:, bass.ds(s * U + u, 1)], neg_r02[:, s],
                                               ALU.add, ALU.min).then_inc(e_ready, 1)
                        dve.wait_ge(e_ready, n + 1)
                        dve.wait_ge(mask_ready, n + 1)
                    m = n - 1
                    if runs(0, 8 * U - 1, m):
                        dve.wait_ge(p_ready, m + 1)
                        v.reciprocal(row_rcp[:, 1 - c:2 - c], row_sum[:, 1 - c:2 - c]).then_inc(rcp_ready, 1)
                    if old:
                        v.bn_aggr(mean_var[:, b2_, :], stats[:, 0, :]).then_inc(mv_ready, 1)
                    if live:
                        v.tensor_tensor_reduce(score[:], score[:], mask[:], 1.0, 3e38, ALU.add, ALU.min,
                                               row_min[:, c:c + 1]).then_inc(score_ready, 1)
                    if s == 1 and runs(0, U - 1, g):
                        dve.wait_ge(mv_ready, 8 * g + 8)
                        v.tensor_scalar(var_eps[:], mean_var[:, :, 1], LN_EPS, None, ALU.add).then_inc(var_ready, 1)
                    if s == LAG + 1 and runs(0, U - 1, g):
                        dve.wait_ge(re_ready, g + 1)
                        await_turns(dve, route_ready, g)
                        v.reciprocal(route_rcp[:], route_sum[:]).then_inc(rr_ready, 1)
                        dve.wait_ge(rr_ready, g + 1)
                        v.tensor_scalar(route[:], route_e[:], route_rcp[:], None, ALU.mult).then_inc(route_ready, 1)
                    ge, e = turn(u, s, LAG)
                    if runs(0, U - 1, ge):
                        k = E * ge + e
                        dve.wait_ge(hi1_ready, k + 1)
                        v.tensor_tensor(a1_lo[:, e % 2], a1[:], a1_hi[:, e % 2].bitcast(F32), ALU.subtract).then_inc(lo1_ready, 1)
                    if s == LAG - 1 and runs(0, U - 1, g):
                        dve.wait_ge(xhi_ready, g + 1)
                        v.tensor_tensor(xT_lo[:], za, xT_hi[:].bitcast(F32), ALU.subtract).then_inc(xlo_ready, 1)
                    if s == LAG and runs(0, U - 1, g):
                        dve.wait_ge(lg_psum, g + 1)
                        await_turns(dve, loff_ready, g)
                        v.scalar_tensor_tensor(logits[:], ob[:, 0:E], 1.0 / B, br_b[:], ALU.mult, ALU.add).then_inc(lg_ready, 1)
                    if s == LAG + 2 and runs(0, U - 1, u - 2):
                        dve.wait_ge(yT_psum, u - 1)
                        slot = x1[:, bass.ds(((u - 2) % 3) * TOK, TOK)]
                        v.tensor_tensor(slot, slot, za, ALU.add).then_inc(out_ready, 1)
                    if s == LAG + 2 and runs(0, U - 1, g):
                        dve.wait_ge(rT_psum, g + 1)
                        v.tensor_copy(routeT[:], ob[0:E, 0:P]).then_inc(rT_ready, 1)
                    if s == LAG + 3 and runs(0, U - 1, g):
                        dve.wait_ge(yc2_psum, g + 1)
                        await_turns(dve, y_ready, g)
                        v.tensor_copy(yc_T[:], ob[:, 0:P]).then_inc(yc2_ready, 1)
                    ge, e = turn(u, s, LAG + 1)
                    if runs(0, U - 1, ge):
                        k = E * ge + e
                        dve.wait_ge(z2_ready, k + 1)
                        await_turns(dve, z3_done, k - 1)
                        if e == 0:
                            dve.wait_ge(rb_ready, ge + 1)
                        v.scalar_tensor_tensor(a2[:, e % 2].rearrange("p (b f) -> p b f", b=B),
                                               zb.rearrange("p (b f) -> p b f", b=B), neg_t2[:, e:e + 1],
                                               route_b[:, e:e + 1, :].to_broadcast([P, B, P]),
                                               ALU.max, ALU.mult).then_inc(a2_ready, 1)
                    if s == LAG + 1 and runs(0, U - 1, u - 2):
                        dve.wait_ge(z3_done, 8 * (u - 1))
                        dve.wait_ge(yc2_ready, u - 1)
                        v.tensor_tensor(xn_y[:].rearrange("p (b f) -> p b f", b=B), yb.rearrange("p (b f) -> p b f", b=B),
                                        yc_T[:].unsqueeze(1).to_broadcast([P, B, P]), ALU.add).then_inc(y_ready, 1)
                    if s == LAG and runs(0, U - 1, g):
                        dve.wait_ge(lg_ready, g + 1)
                        v.reduce_max(logit_max[:], logits[:], AX_X).then_inc(lmax_ready, 1)
                        dve.wait_ge(lmax_ready, g + 1)
                        v.tensor_scalar(logit_off[:], logits[:], logit_max[:], None, ALU.subtract).then_inc(loff_ready, 1)

            over_groups(dve, iteration, U + 1)

        @block.tensor
        def _(pe):
            mm = nc.tensor.matmul
            pe.wait_ge(ident_ready, 1)
            pe.wait_ge(gnn_loaded, 32)
            nc.tensor.transpose(bank[:, 6, 0:D], W_sb[:], ident[:]).then_inc(WT_psum, 1)
            mm(bank[:, 0, 0:2], W_sb[:], a_cols[:], start=True, stop=True)
            mm(bank[:, 1, 0:P], W_sb[:], a_cols[:, 1:2].to_broadcast([P, P]), start=True, stop=True).then_inc(wl_psum, 1)
            for b in range(B):
                pe.wait_ge(pxn, b + 1)
                if b == 0:
                    pe.wait_ge(WT_ready, 1)
                    pe.wait_ge(wl_ready, 2)
                else:
                    pe.wait_ge(pTc, b)
                for t in range(NT):
                    last = nc.tensor.transpose(za[:, t * P:(t + 1) * P], pro_xn[:, t * D:(t + 1) * D], ident[:])
                last.then_inc(pT, 1)
                pe.wait_ge(pTc, b + 1)
                if b >= 1:
                    pe.wait_ge(phc, b)
                    pe.wait_ge(pl, b)
                for t in range(NT):
                    last = mm(pro_h[:, t, 0:D + 1], pro_xnT[:, t * P:(t + 1) * P], W_aug[:, 0:D + 1], start=True, stop=True)
                last.then_inc(ph, 1)
                if b >= 1:
                    pe.wait_ge(prc, b)
                for i in range(2):
                    last = mm(pro_r[:, i * HALF:(i + 1) * HALF], wr_bc[:], pro_xnT[:, i * HALF:(i + 1) * HALF], start=True, stop=True)
                last.then_inc(pr, 1)
            pe.wait_ge(prm_loaded, 16 * 10)
            pe.wait_ge(pTc, B)
            nc.tensor.transpose(bank[:, 1, 0:P], prm_rows[:], ident[:]).then_inc(prm_psum, 1)
            pe.wait_ge(bn_step, 7)
            pe.wait_ge(prc, B)
            for e in range(E):
                last = mm(pro_r[:, e * P:(e + 1) * P], bn_s[:, E + e:E + e + 1].to_broadcast([P, P]), ident[:], start=True, stop=True)
            last.then_inc(s2_psum, 1)
            pe.wait_ge(w_loaded, 16 * 6)
            for e in range(E):
                mm(bank[0:E, 0, 0:D], t2_diag[:, e * E:(e + 1) * E], Wo_sb[:, e, :], start=(e == 0), stop=False)
            mm(bank[0:E, 0, 0:D], ident[0:E, 0:E], bo_sb[:], start=False, stop=True).then_inc(yc_psum, 1)
            pe.wait_ge(wsplit, 3)
            pe.wait_ge(yc_ready, 1)
            pe.wait_ge(phc, B)
            pe.wait_ge(pl, B)

            def three(z, w_hi, w_lo, a_hi, a_lo):
                for w, a, first, final in ((w_hi, a_hi, True, False), (w_hi, a_lo, False, False), (w_lo, a_hi, False, True)):
                    for i in range(2):
                        last = mm(z[:, i * HALF:(i + 1) * HALF], w, a[:, i * HALF:(i + 1) * HALF], start=first, stop=final)
                return last

            def transpose_group(src, done):
                for b in range(B):
                    last = nc.tensor.transpose(za[:, b * P:(b + 1) * P], src[:, b * P:(b + 1) * P], ident[:])
                last.then_inc(done, 1)

            def layer1(u, s):
                g, e = turn(u, s, LAG)
                if not runs(0, U - 1, g):
                    return None
                k = E * g + e
                if e == 0:
                    pe.wait_ge(xlo_ready, g + 1)
                if s == LAG + 2 and runs(0, U - 1, u - 1):
                    pe.wait_ge(rb_ready, u)
                if s == LAG + 3 and runs(0, U - 1, u - 2):
                    pe.wait_ge(out_ready, u - 1)
                await_turns(pe, a1_ready, k)
                w = slice(e * H, (e + 1) * H)
                three(za, W1_hi[:, w], W1_lo[:, w], xT_hi[:], xT_lo[:]).then_inc(z1_ready, 1)
                return k

            def transpose_probs(u, s, half):
                m = 8 * u + s - 1
                if not runs(0, 8 * U - 1, m):
                    return
                if half == 0:
                    pe.wait_ge(p_ready, m + 1)
                await_turns(pe, pt_copied, 2 * m + half)
                for t in range(4):
                    q = 4 * half + t
                    last = nc.tensor.transpose(ptb[:, t * P:(t + 1) * P], probs[:, q * P:(q + 1) * P], ident[:])
                last.then_inc(pt_psum, 1)

            def layer3(u, s):
                g, e = turn(u, s, LAG + 2)
                if not runs(0, U - 1, g):
                    return
                k = E * g + e
                pe.wait_ge(a2_ready, k + 1)
                if e == 0:
                    await_turns(pe, y_ready, g)
                for i in range(2):
                    last = mm(yb[:, i * HALF:(i + 1) * HALF], Wo_sb[:, e, :], a2[:, e % 2, i * HALF:(i + 1) * HALF],
                              start=(e == 0), stop=(e == E - 1))
                last.then_inc(z3_done, 1)

            def layer2(u, s):
                g, e = turn(u, s, LAG + 1)
                if not runs(0, U - 1, g):
                    return
                k = E * g + e
                pe.wait_ge(lo1_ready, k + 1)
                await_turns(pe, a2_ready, k)
                w = slice(e * H, (e + 1) * H)
                three(zb, W2_hi[:, w], W2_lo[:, w], a1_hi[:, e % 2], a1_lo[:, e % 2]).then_inc(z2_ready, 1)

            def attend(u, s):
                m = 8 * u + s - 1
                b = (s - 1) % 8
                if not runs(0, 8 * U - 1, m):
                    return
                g = u - 1
                pe.wait_ge(pt_copied, 2 * m + 2)
                await_turns(pe, x1_ready, m)
                if s == LAG and runs(0, U - 1, g):
                    pe.wait_ge(lg_ready, g + 1)
                if s == LAG + 2 and runs(0, U - 1, g):
                    pe.wait_ge(rT_ready, g + 1)
                if s == LAG + 3 and runs(0, U - 1, g):
                    pe.wait_ge(yc2_ready, g + 1)
                for t in range(NT):
                    last = mm(ob[:, 0:D], probsT[:, t, :], h_all[:, b, t, :], start=(t == 0), stop=(t == NT - 1))
                last.then_inc(o_ready, 1)

            def iteration(u):
                for s in range(8):
                    if isinstance(u, int) and u > U and s > 5:
                        break
                    g = u - 1
                    k1 = layer1(u, s)
                    transpose_probs(u, s, 0)
                    layer3(u, s)
                    transpose_probs(u, s, 1)
                    if s in (LAG - 1, LAG + 1, LAG + 2) and k1 is not None:
                        pe.wait_ge(a1_ready, k1 + 1)
                    if s == LAG - 1 and runs(0, U - 1, g):
                        pe.wait_ge(xn_ready, g + 1)
                        transpose_group(xn_y, xT_psum)
                    if s == LAG + 1 and runs(0, U - 1, g):
                        pe.wait_ge(route_ready, g + 1)
                        for e in range(E):
                            last = mm(za[:, e * P:(e + 1) * P], route[:, e:e + 1].to_broadcast([P, P]), ident[:], start=True, stop=True)
                        last.then_inc(rb_psum, 1)
                    if s == LAG + 2 and runs(0, U - 1, u - 2):
                        pe.wait_ge(y_ready, u - 1)
                        transpose_group(xn_y, yT_psum)
                    if s in (LAG, LAG + 2, LAG + 3) and runs(0, U - 1, g):
                        await_turns(pe, x1_ready, 8 * u + s - 1 if runs(0, 8 * U, 8 * u + s - 1) else 8 * U)
                    if s == LAG and runs(0, U - 1, g):
                        first = True
                        for w, a in ((Wr_hi, xT_hi), (Wr_hi, xT_lo), (Wr_lo, xT_hi)):
                            for b in range(B):
                                final = w is Wr_lo and b == B - 1
                                last = mm(ob[:, 0:E], a[:, b * P:(b + 1) * P], w[:], start=first, stop=final)
                                first = False
                        last.then_inc(lg_psum, 1)
                    if s == LAG + 2 and runs(0, U - 1, g):
                        mm(ob[0:E, 0:P], route[:], ident[:], start=True, stop=True).then_inc(rT_psum, 1)
                    if s == LAG + 3 and runs(0, U - 1, g):
                        pe.wait_ge(rT_ready, g + 1)
                        mm(ob[:, 0:P], y_const[:], routeT[:], start=True, stop=True).then_inc(yc2_psum, 1)
                    layer2(u, s)
                    attend(u, s)

            over_groups(pe, iteration, U + 1)


_INS = ["x", "adj", "L0_gnn_W", "L0_gnn_a", "L0_ffn_Wr", "L0_ffn_br", "L0_ffn_W1", "L0_ffn_b1", "L0_ffn_g1",
        "L0_ffn_be1", "L0_ffn_m1", "L0_ffn_v1", "L0_ffn_W2", "L0_ffn_b2", "L0_ffn_g2", "L0_ffn_be2", "L0_ffn_m2",
        "L0_ffn_v2", "L0_ffn_Wo", "L0_ffn_bo"]


def kernel(**inputs):
    import numpy as np
    import concourse.bacc as bacc
    from concourse.bass_utils import run_bass_kernel_spmd

    nc = bacc.Bacc("TRN2", target_bir_lowering=False, num_devices=1)
    arrays, args = {}, []
    for name in _INS:
        a = np.ascontiguousarray(inputs[name])
        arrays["in_" + name] = a
        args.append(nc.dram_tensor("in_" + name, a.shape, mybir.dt.from_np(a.dtype), kind="ExternalInput").ap())
    out = nc.dram_tensor("out_0", arrays["in_x"].shape, F32, kind="ExternalOutput").ap()
    gat_moe(nc, *args, out)
    r = run_bass_kernel_spmd(nc, [arrays], core_ids=[0])
    return r.results[0]["out_0"]
```
